# Optimizing a Trainium2 kernel written in Bass

```python
import numpy as np
import jax
import jax.numpy as jnp

def _softmax(x, axis=-1):
    return jax.nn.softmax(x, axis=axis)
def _gelu(x):
    return jax.nn.gelu(x, approximate=True)
def _silu(x):
    return jax.nn.silu(x)
def _sigmoid(x):
    return jax.nn.sigmoid(x)
def _layernorm(x, axis=-1, eps=1e-5):
    m = jnp.mean(x, axis=axis, keepdims=True)
    v = jnp.var(x, axis=axis, keepdims=True)
    return (x - m) / jnp.sqrt(v + eps)
def _scatter_add(tgt, idx, src, axis=0):
    return tgt.at[idx].add(src)
def _segment_sum(src, seg, n):
    return jax.ops.segment_sum(src, seg, n)

kernel_name = 'mk_adj_preln_d1_adj_64_278616'

def setup_inputs(seed: int = 0):
    np.random.seed(seed)
    _w = jnp.asarray
    def _rec_inputs():
        import jax
        import jax.numpy as jnp
        _gk = jax.random.key(seed)
        x = -9.806e-05 + 1 * jax.random.normal(jax.random.fold_in(_gk, 1), (4096, 64), jnp.float32)
        _a = jax.random.bernoulli(jax.random.fold_in(_gk, 2), 0.000976562, (4096, 4096))
        _af = _a.astype(jnp.float32)
        adj = _af
        return x, adj
    x, adj = _rec_inputs()
    def _L0_gnn_setup():
        import jax, jax.numpy as jnp
        import numpy as np
        N, D_IN, D_OUT = (8192, 64, 64)
        MAX_NEIGH = 100
        DECAY = 0.5
        key = jax.random.key(seed)
        k1, k2, k3, k4 = jax.random.split(key, 4)
        stdv = 1.0 / np.sqrt(D_OUT)
        inputs = {'input': jax.random.normal(k1, (N, D_IN), dtype=jnp.float32), 'adj': jax.random.randint(k2, (N, N), 0, 2).astype(jnp.float32), 'weight': jax.random.uniform(k3, (D_IN, D_OUT), minval=-stdv, maxval=stdv, dtype=jnp.float32), 'bias': jax.random.uniform(k4, (D_OUT,), minval=-stdv, maxval=stdv, dtype=jnp.float32)}
        return inputs
    _L0_gnn_all = _L0_gnn_setup()
    _L0_gnn_in = {k: v for k, v in _L0_gnn_all.items() if k in ('weight', 'bias', )}
    del _L0_gnn_all

    return {
        "x": x,
        "adj": adj,
        "L0_gnn_weight": _L0_gnn_in["weight"],
        "L0_gnn_bias": _L0_gnn_in["bias"],
    }

def reference(x, adj, L0_gnn_weight, L0_gnn_bias):
    import jax
    import jax.numpy as jnp
    def _L0_gnn_ref(input, adj, weight, bias):
        import jax, jax.numpy as jnp
        import numpy as np
        N, D_IN, D_OUT = (8192, 64, 64)
        MAX_NEIGH = 100
        DECAY = 0.5
        support = input @ weight
        mask = (adj != 0).astype(support.dtype)
        rank = jnp.cumsum(mask, axis=1)
        deg = rank[:, -1:]
        k = jnp.minimum(deg, float(MAX_NEIGH))
        pos = rank - (deg - k)
        w = mask * jnp.where(pos > 0, DECAY ** (k - pos), 0.0)
        out = w @ support + bias
        return out

    h = jnp.maximum(_layernorm(x, axis=-1), 0.0)
    x = x + _L0_gnn_ref(h, adj, L0_gnn_weight, L0_gnn_bias)
    return x


_drawn_inputs = setup_inputs


def setup_inputs(seed=0):
    import zlib

    import numpy as np

    out = dict(_drawn_inputs(seed))
    spreads = {}
    factors = {}
    for name, (base, spread) in spreads.items():
        noise = np.random.default_rng([zlib.crc32(name.encode()), seed]).standard_normal(out[name].shape)
        drawn = base * np.exp(spread * noise) if base else spread * noise
        out[name] = jnp.asarray(drawn.astype(out[name].dtype))
    for name, factor in factors.items():
        out[name] = (out[name] * factor).astype(out[name].dtype)
    return out
```

```python
from contextlib import ExitStack

import concourse.bass as bass
from concourse import mybir
from concourse.alu_op_type import AluOpType as ALU

P = 128
MAX_NEIGH = 100
EPS = 1e-5
PARTS = 3


def decayed_neighbour_layer(nc, x, adj, weight, bias, out):
    F32, BF16, I16 = mybir.dt.float32, mybir.dt.bfloat16, mybir.dt.int16
    ACT = mybir.ActivationFunctionType
    X = mybir.AxisListType.X

    N, D = x.shape
    BLOCKS = N // P
    TILES = 8
    GROUPS = 2
    GT = TILES // GROUPS
    GR = GT * P
    ROWS = TILES * P
    SUPERS = N // ROWS
    CB = 4
    CC = CB * P
    CHUNKS = BLOCKS // CB
    LB = 8
    LOOPS = BLOCKS // LB
    LEAD = 5
    W3 = PARTS * D
    ONE = 1 << 7
    SHIFT = 127 - MAX_NEIGH
    QB = BLOCKS // 4

    ctx = ExitStack()
    with ctx:
        def sb(name, shape, dt):
            return ctx.enter_context(nc.sbuf_tensor(name, shape, dt))

        def sem(name):
            return ctx.enter_context(nc.semaphore(name))

        adj_sb = sb("adj_sb", [P, 2, TILES, CC], F32)
        nat = sb("nat", [P, 2, TILES, CC], BF16)
        mask_t = sb("mask_t", [P, 2, GROUPS, GR, 2], BF16)
        wts = sb("wts", [P, 2, ROWS], BF16)
        sp = sb("sp", [P, BLOCKS, W3], BF16)
        x_sb = sb("x_sb", [P, BLOCKS, D], F32)
        xb = sb("xb", [P, BLOCKS * D], F32)
        xc = sb("xc", [P, BLOCKS, D], F32)
        h = sb("h", [P, BLOCKS, D], F32)
        h_t = sb("h_t", [D, BLOCKS, P], F32)
        sup = sb("sup", [P, BLOCKS, D], F32)
        red = sb("red", [P, TILES, D], F32)
        out_sb = sb("out_sb", [P, BLOCKS * D], F32)
        stat = sb("stat", [P, 8, BLOCKS], F32)
        bias_sb = sb("bias_sb", [P, D], F32)
        w_sb = sb("w_sb", [D, D], F32)
        ident = sb("ident", [P, P], F32)
        cnt_w = sb("cnt_w", [P, P], BF16)
        car_w = sb("car_w", [P, P], BF16)

        tr_ps = ctx.enter_context(nc.psum_tensor("tr_ps", [P, GROUPS, 512], F32))
        cnt_ps = ctx.enter_context(nc.psum_tensor("cnt_ps", [P, GROUPS, 512], F32))
        acc_ps = ctx.enter_context(nc.psum_tensor("acc_ps", [P, TILES // 2, 512], F32))

        x_landed = sem("x_landed")
        small_landed = sem("small_landed")
        adj_landed = [sem("adj_landed0"), sem("adj_landed1")]
        out_landed = sem("out_landed")
        const_step = sem("const_step")
        const_ready = sem("const_ready")
        pre_dve = sem("pre_dve")
        pre_act = sem("pre_act")
        h_transposed = sem("h_transposed")
        ht_ready = sem("ht_ready")
        sup_product = sem("sup_product")
        hi_ready = sem("hi_ready")
        parts_ready = sem("parts_ready")
        nat_ready = sem("nat_ready")
        tr_done = sem("tr_done")
        mask_ready = sem("mask_ready")
        counted = sem("counted")
        wts_ready = sem("wts_ready")
        carried = sem("carried")
        product_done = sem("product_done")
        acc_read = sem("acc_read")
        out_ready = sem("out_ready")

        block = ctx.enter_context(nc.Block())

        @block.sync
        def _(sp_):
            sp_.dma_start(x_sb[:], x.rearrange("(b p) d -> p b d", p=P)).then_inc(x_landed, 16)

            def load(row0, c):
                rows = adj[bass.ds(row0, ROWS), N - (c + 1) * CC:N - c * CC]
                sp_.dma_start(adj_sb[:, c % 2], rows.rearrange("(t p) c -> p t c", p=P)).then_inc(adj_landed[c % 2], 16)

            with sp_.Fori(0, SUPERS) as s:
                row0 = sp_.snap(s * ROWS)
                for c in range(CHUNKS):
                    sp_.wait_ge(nat_ready, s * (CHUNKS * 4) + c * 4)
                    sp_.nop(nofuse=True)
                    load(row0, c)
            for i in range(2):
                sp_.wait_ge(adj_landed[i], 16 * SUPERS * CHUNKS // 2)
                sp_.sem_inc(adj_landed[i], 16)

        @block.gpsimd
        def _(pool):
            pool.dma_start(w_sb[:], weight).then_inc(small_landed, 16)
            pool.dma_start(bias_sb[:], bias.rearrange("(a d) -> a d", a=1).broadcast_to([P, D])).then_inc(small_landed, 16)
            pool.memset(ident[:], 0.0).then_inc(const_step, 1)
            pool.memset(cnt_w[:], -float(ONE)).then_inc(const_step, 1)
            pool.memset(car_w[:], 0.0).then_inc(const_step, 1)
            pool.wait_ge(const_step, 3)
            pool.affine_select(out=ident[:], in_=ident[:], compare_op=ALU.not_equal, fill=1.0, base=0,
                               pattern=[[-1, P]], channel_multiplier=1).then_inc(const_step, 1)
            pool.affine_select(out=cnt_w[:], in_=cnt_w[:], compare_op=ALU.is_gt, fill=0.0, base=0,
                               pattern=[[-1, P]], channel_multiplier=1).then_inc(const_step, 1)
            pool.affine_select(out=car_w[:], in_=car_w[:], compare_op=ALU.is_gt, fill=-float(ONE), base=0,
                               pattern=[[-1, P]], channel_multiplier=1).then_inc(const_step, 1)
            pool.wait_ge(const_step, 6)
            pool.affine_select(out=cnt_w[:], in_=cnt_w[:], compare_op=ALU.not_equal, fill=float(MAX_NEIGH * ONE), base=0,
                               pattern=[[-1, P]], channel_multiplier=1).then_inc(const_ready, 1)
            pool.affine_select(out=car_w[:], in_=car_w[:], compare_op=ALU.not_equal, fill=-float((MAX_NEIGH + 1) * ONE),
                               base=0, pattern=[[-1, P]], channel_multiplier=1).then_inc(const_ready, 1)
            with pool.Fori(0, SUPERS) as s:
                row0, col0 = pool.snap(s * ROWS), pool.snap(s * (TILES * D))
                pool.wait_ge(out_ready, s + 1)
                pool.nop(nofuse=True)
                pool.dma_start(out[bass.ds(row0, ROWS), :].rearrange("(t p) d -> p t d", p=P),
                               out_sb[:, bass.ds(col0, TILES * D)].rearrange("p (t d) -> p t d", d=D)
                               ).then_inc(out_landed, 16)
            pool.wait_ge(out_landed, 16 * SUPERS)

        @block.scalar
        def _(act):
            act.wait_ge(pre_dve, 3)
            act.activation(h[:], xc[:], ACT.Square).then_inc(pre_act, 1)
            act.wait_ge(pre_dve, 5)
            act.activation(stat[:, 3], stat[:, 2], ACT.Sqrt).then_inc(pre_act, 1)
            for e in range(4):
                for i in range(2):
                    b0 = e * QB + i * 4
                    act.wait_ge(h_transposed, 2 * e + i + 1)
                    act.activation(h_t[:, b0:b0 + 4], acc_ps[0:D, i].rearrange("p (t r) -> p t r", r=P), ACT.Relu
                                   ).then_inc(ht_ready, 1)
                act.wait_ge(sup_product, e + 1)
                act.activation(sp[:, e * QB:(e + 1) * QB, 0:D], acc_ps[:, 2 + e % 2].rearrange("p (b d) -> p b d", d=D),
                               ACT.Copy, scale=float(2 ** SHIFT)).then_inc(hi_ready, 1)

            def encode(n0, t):
                for g in range(GROUPS):
                    act.wait_ge(counted, 2 * n0 + 2 * t + g + 1)
                    if g == 0:
                        act.wait_ge(product_done, n0 + t)
                    act.activation(wts[:, t % 2, g * GR:(g + 1) * GR].bitcast(I16), cnt_ps[:, g], ACT.Relu
                                   ).then_inc(wts_ready, 1)

            with act.Fori(0, SUPERS) as s:
                with act.Fori(0, LOOPS) as q:
                    for t in range(LB):
                        encode(s * BLOCKS + q * LB, t)

        @block.vector
        def _(dve):
            dve.sem_inc(nat_ready, 4)

            def natural(n0, t):
                k, i = t // 4, t % 4
                dve.wait_ge(adj_landed[k % 2], n0 * 2 + 16 * (k // 2 + 1))
                if k >= 1:
                    dve.wait_ge(tr_done, n0 + 4 * k - 4 + i // 2)
                src = adj_sb[:, k % 2, 2 * i:2 * i + 2].rearrange("p t (pr h w) -> p (t pr) h w", h=2, w=P)
                dst = nat[:, k % 2, 2 * i:2 * i + 2].rearrange("p t (pr w h) -> p (t pr) h w", h=2, w=P)
                dve.tensor_scalar(dst, src, 0.0, None, ALU.not_equal).then_inc(nat_ready, 1)

            def evacuate(n0, t):
                p, g = t // 2, t % 2
                dve.wait_ge(tr_done, n0 + t + 2)
                if p >= 1:
                    dve.wait_ge(carried, n0 * 2 + 4 * p - 4 + g)
                dve.tensor_copy(mask_t[:, p % 2, g], tr_ps[:, g].bitcast(BF16).rearrange("p (r h) -> p r h", h=2)
                                ).then_inc(mask_ready, 1)

            dve.wait_ge(x_landed, 16)
            dve.tensor_reduce(stat[:, 0], x_sb[:], X, ALU.add).then_inc(pre_dve, 1)
            dve.wait_ge(pre_dve, 1)
            dve.tensor_scalar(stat[:, 1], stat[:, 0], 1.0 / D, None, ALU.mult).then_inc(pre_dve, 1)
            dve.wait_ge(pre_dve, 2)
            dve.tensor_tensor(xc[:], x_sb[:], bcast(stat[:, 1], D), ALU.subtract).then_inc(pre_dve, 1)
            dve.wait_ge(pre_act, 1)
            dve.tensor_reduce(stat[:, 0], h[:], X, ALU.add).then_inc(pre_dve, 1)
            dve.wait_ge(pre_dve, 4)
            dve.tensor_scalar(stat[:, 2], stat[:, 0], 1.0 / D, EPS, ALU.mult, ALU.add).then_inc(pre_dve, 1)
            dve.wait_ge(pre_act, 2)
            dve.reciprocal(stat[:, 4], stat[:, 3]).then_inc(pre_dve, 1)
            dve.wait_ge(pre_dve, 6)
            dve.tensor_tensor(stat[:, 5], stat[:, 4], stat[:, 4], ALU.mult).then_inc(pre_dve, 1)
            dve.wait_ge(pre_dve, 7)
            dve.tensor_tensor(stat[:, 6], stat[:, 5], stat[:, 2], ALU.mult).then_inc(pre_dve, 1)
            dve.wait_ge(pre_dve, 8)
            dve.tensor_scalar(stat[:, 5], stat[:, 6], -0.5, 1.5, ALU.mult, ALU.add).then_inc(pre_dve, 1)
            dve.wait_ge(pre_dve, 9)
            dve.tensor_tensor(stat[:, 7], stat[:, 5], stat[:, 4], ALU.mult).then_inc(pre_dve, 1)
            dve.wait_ge(pre_dve, 10)
            dve.tensor_tensor(h[:], xc[:], bcast(stat[:, 7], D), ALU.mult).then_inc(pre_dve, 1)
            for t in range(LEAD):
                natural(0, t)
            dve.wait_ge(small_landed, 32)
            dve.tensor_tensor(xb[:].rearrange("p (b d) -> p b d", d=D), x_sb[:], bcast_mid(bias_sb[:], BLOCKS), ALU.add)
            for e in range(4):
                blk = slice(e * QB, (e + 1) * QB)
                dve.wait_ge(hi_ready, e + 1)
                dve.tensor_scalar(sup[:, blk], acc_ps[:, 2 + e % 2].rearrange("p (b d) -> p b d", d=D),
                                  float(2 ** SHIFT), None, ALU.mult).then_inc(parts_ready, 1)
                dve.wait_ge(parts_ready, 4 * e + 1)
                dve.tensor_tensor(sup[:, blk], sup[:, blk], sp[:, blk, 0:D], ALU.subtract).then_inc(parts_ready, 1)
                dve.wait_ge(parts_ready, 4 * e + 2)
                dve.tensor_copy(sp[:, blk, D:2 * D], sup[:, blk]).then_inc(parts_ready, 1)
                dve.wait_ge(parts_ready, 4 * e + 3)
                dve.tensor_tensor(sp[:, blk, 2 * D:W3], sup[:, blk], sp[:, blk, D:2 * D], ALU.subtract
                                  ).then_inc(parts_ready, 1)

            for t in range(2):
                evacuate(0, t)
            with dve.Fori(0, SUPERS) as s:
                with dve.Fori(0, LOOPS) as q:
                    for t in range(LB):
                        natural(s * BLOCKS + q * LB, t + LEAD)
                        evacuate(s * BLOCKS + q * LB, t + 2)
                cols = bass.ds(dve.snap(s * (TILES * D)), TILES * D)
                dve.wait_ge(product_done, s * BLOCKS + BLOCKS + 1)
                dve.wait_ge(out_ready, s)
                for a in range(TILES // 2):
                    dve.tensor_reduce(red[:, 2 * a:2 * a + 2],
                                      acc_ps[:, a, 0:2 * W3].rearrange("p (t k d) -> p t d k", t=2, d=D),
                                      X, ALU.add).then_inc(acc_read, 1)
                dve.wait_ge(acc_read, s * (TILES // 2) + TILES // 2)
                dve.tensor_tensor(out_sb[:, cols], red[:].rearrange("p t d -> p (t d)"), xb[:, cols], ALU.add
                                  ).then_inc(out_ready, 1)

        @block.tensor
        def _(pe):
            pe.sem_inc(tr_done, 1)
            pe.sem_inc(carried, 1)
            pe.sem_inc(product_done, 1)
            pe.wait_ge(pre_dve, 11)
            pe.wait_ge(const_ready, 2)
            pe.wait_ge(small_landed, 32)
            for e in range(4):
                for i in range(2):
                    if e:
                        pe.wait_ge(ht_ready, 2 * e + i - 1)
                    for t in range(4):
                        last = pe.transpose(acc_ps[0:D, i, t * P:(t + 1) * P], h[:, BLOCKS - 1 - (e * QB + i * 4 + t)], ident[:])
                    last.then_inc(h_transposed, 1)
                pe.wait_ge(ht_ready, 2 * e + 2)
                if e >= 2:
                    pe.wait_ge(hi_ready, e - 1)
                    pe.wait_ge(parts_ready, 4 * (e - 2) + 1)
                for t in range(QB):
                    last = pe.matmul(acc_ps[:, 2 + e % 2, t * D:(t + 1) * D], h_t[:, e * QB + t], w_sb[:],
                                     start=True, stop=True)
                last.then_inc(sup_product, 1)

            def transpose(n0, t):
                k, pr, g = t // 4, 1 - t // 2 % 2, t % 2
                pe.wait_ge(nat_ready, n0 + 4 * k + 2 * g + 6)
                if t >= 2:
                    pe.wait_ge(mask_ready, n0 + t - 1)
                for i in range(GT):
                    words = nat[:, k % 2, g * GT + i, pr * 2 * P:(pr + 1) * 2 * P].bitcast(F32)
                    last = pe.transpose(tr_ps[:, g, i * P:(i + 1) * P], words, ident[:])
                last.then_inc(tr_done, 1)

            def masks(t, g):
                return mask_t[:, t // 2 % 2, g, :, 1 - t % 2]

            def count(n0, t, first):
                for g in range(GROUPS):
                    pe.wait_ge(mask_ready, n0 + 2 * (t // 2) + g + 1)
                    pe.matmul(cnt_ps[:, g], cnt_w[:], masks(t, g), start=first, stop=True,
                              skip_group_check=True).then_inc(counted, 1)

            def carry(n0, t):
                for g in range(GROUPS):
                    pe.wait_ge(wts_ready, 2 * n0 + 2 * t + g + 1)
                    pe.matmul(cnt_ps[:, g], car_w[:], masks(t, g), start=False, stop=True,
                              skip_group_check=True).then_inc(carried, 1)

            def product(o, t, first):
                for i in range(TILES):
                    rhs = sp[:, o].rearrange("p a n -> p (a n)") if not isinstance(o, int) else sp[:, o]
                    last = pe.matmul(acc_ps[:, i // 2, (i % 2) * W3:(i % 2 + 1) * W3],
                                     wts[:, t % 2, i * P:(i + 1) * P], rhs,
                                     start=first and i % 2 == 0, stop=True, skip_group_check=True)
                last.then_inc(product_done, 1)
                return last

            for t in range(2):
                transpose(0, t)
            pe.wait_ge(parts_ready, 16)
            with pe.Fori(0, SUPERS) as s:
                for t in range(LB):
                    n0 = s * BLOCKS
                    count(n0, t, t == 0)
                    transpose(n0, t + 2)
                    if t == 1:
                        pe.wait_ge(acc_read, s * (TILES // 2))
                    if t:
                        product(t - 1, t - 1, t == 1)
                    carry(n0, t)
                with pe.Fori(1, LOOPS) as q:
                    n0 = s * BLOCKS + q * LB
                    for t in range(LB):
                        count(n0, t, False)
                        transpose(n0, t + 2)
                        product(bass.ds(q * LB + (t - 1), 1), t - 1, False)
                        carry(n0, t)
                product(BLOCKS - 1, BLOCKS - 1, False)


def bcast(ap, n):
    return ap.unsqueeze(2).broadcast_to([ap.shape[0], ap.shape[1], n])


def bcast_mid(ap, n):
    return ap.unsqueeze(1).broadcast_to([ap.shape[0], n, ap.shape[1]])


_INS = ["x", "adj", "L0_gnn_weight", "L0_gnn_bias"]


def kernel(**inputs):
    import numpy as np
    import concourse.bacc as bacc
    from concourse.bass_utils import run_bass_kernel_spmd as run

    nc = bacc.Bacc("TRN2", target_bir_lowering=False, num_devices=1)
    arrays, args = {}, []
    for name in _INS:
        a = np.ascontiguousarray(inputs[name])
        arrays[f"in_{name}"] = a
        args.append(nc.dram_tensor(f"in_{name}", a.shape, mybir.dt.from_np(a.dtype), kind="ExternalInput").ap())
    args.append(nc.dram_tensor("out_x", inputs["x"].shape, mybir.dt.float32, kind="ExternalOutput").ap())
    decayed_neighbour_layer(nc, *args)
    return run(nc, [arrays], core_ids=[0]).results[0]["out_x"]
```

```python
from contextlib import ExitStack

import concourse.bass as bass
from concourse import mybir
from concourse.alu_op_type import AluOpType as ALU

P = 128
MAX_NEIGH = 100
EPS = 1e-5
PARTS = 3


def decayed_neighbour_layer(nc, x, adj, weight, bias, out):
    F32, BF16, I16 = mybir.dt.float32, mybir.dt.bfloat16, mybir.dt.int16
    ACT = mybir.ActivationFunctionType
    X = mybir.AxisListType.X

    N, D = x.shape
    TILES = 8
    GROUPS = 2
    GT = TILES // GROUPS
    GR = GT * P
    ROWS = TILES * P
    SUPERS = N // ROWS
    BC = P - 1
    BLOCKS = N // BC
    TAIL = N - BLOCKS * BC
    CB = 2
    BUFS = 4
    CHUNKS = BLOCKS // CB
    CW = TAIL + CB * BC
    LB = BUFS * CB
    LOOPS = BLOCKS // LB
    ALL = BLOCKS + 1
    STEPS = GROUPS * ALL
    W3 = PARTS * D
    ONE = 1 << 7
    FULL = MAX_NEIGH * ONE
    SHIFT = 127 - MAX_NEIGH
    XT = N // P
    SETS = [(b, LB) for b in range(BLOCKS - LB, -1, -LB)] + [(BLOCKS, 1)]
    HALVES = [(b, LB // 2) for b in range(BLOCKS - LB // 2, -1, -LB // 2)] + [(BLOCKS, 1)]
    assert TAIL == 32 and BLOCKS % LB == 0

    ctx = ExitStack()
    with ctx:
        def sb(name, shape, dt):
            return ctx.enter_context(nc.sbuf_tensor(name, shape, dt))

        def sem(name):
            return ctx.enter_context(nc.semaphore(name))

        adj_sb = sb("adj_sb", [P, BUFS, TILES, CW], F32)
        mask_t = sb("mask_t", [P, 2, ROWS], BF16)
        mask_tail = sb("mask_tail", [P, ROWS], BF16)
        wts = sb("wts", [P, 2, ROWS], BF16)
        wts_tail = sb("wts_tail", [P, ROWS], BF16)
        sp = sb("sp", [P, ALL, W3], BF16)
        xs = sb("xs", [P, ALL, D], F32)
        xb = sb("xb", [P, XT * D], F32)
        xc = sb("xc", [P, ALL, D], F32)
        sq = sb("sq", [P, ALL, D], F32)
        h_t = sb("h_t", [D, ALL, P], F32)
        sup = sb("sup", [P, ALL, D], F32)
        red = sb("red", [P, TILES, D], F32)
        out_sb = sb("out_sb", [P, XT * D], F32)
        stat = sb("stat", [P, 8, ALL], F32)
        bias_sb = sb("bias_sb", [P, D], F32)
        w_sb = sb("w_sb", [D, D], F32)
        ident = sb("ident", [P, P], F32)
        ident_h = sb("ident_h", [P, P], BF16)
        cnt_w = sb("cnt_w", [P, P], BF16)
        cnt_tail = sb("cnt_tail", [P, P], BF16)

        tr_ps = [ctx.enter_context(nc.psum_tensor(f"tr_ps{g}", [P, 1024], BF16)) for g in range(GROUPS)]
        cnt_ps = ctx.enter_context(nc.psum_tensor("cnt_ps", [P, GROUPS, 512], F32))
        acc_ps = ctx.enter_context(nc.psum_tensor("acc_ps", [P, TILES // 2, 512], F32))

        x_zeroed = sem("x_zeroed")
        x_landed = sem("x_landed")
        x_tail_landed = sem("x_tail_landed")
        small_landed = sem("small_landed")
        adj_landed = [sem(f"adj_landed{i}") for i in range(BUFS)]
        out_landed = sem("out_landed")
        const_step = sem("const_step")
        ident_ready = sem("ident_ready")
        const_ready = sem("const_ready")
        w_landed = sem("w_landed")
        norm_step = sem("norm_step")
        root_ready = sem("root_ready")
        xc_transposed = sem("xc_transposed")
        ht_ready = sem("ht_ready")
        sup_product = sem("sup_product")
        sup_ready = sem("sup_ready")
        split_step = [sem("split_step0"), sem("split_step1")]
        first_parts_ready = sem("first_parts_ready")
        more_parts_ready = sem("more_parts_ready")
        tr_done = sem("tr_done")
        mask_ready = sem("mask_ready")
        carry_ready = sem("carry_ready")
        counted = sem("counted")
        wts_ready = sem("wts_ready")
        product_done = sem("product_done")
        acc_read = sem("acc_read")
        out_ready = sem("out_ready")

        block = ctx.enter_context(nc.Block())

        def split(eng, who, e, k):
            step = split_step[who]
            blk = slice(SETS[e][0], sum(SETS[e]))
            eng.wait_ge(sup_ready, e + 1)
            eng.tensor_tensor(sup[:, blk], sup[:, blk], per_row(stat[:, 7, blk], D), ALU.mult).then_inc(step, 1)
            eng.wait_ge(step, 4 * k + 1)
            eng.tensor_copy(sp[:, blk, 0:D], sup[:, blk]).then_inc(step, 1)
            eng.wait_ge(step, 4 * k + 2)
            eng.tensor_tensor(sup[:, blk], sup[:, blk], sp[:, blk, 0:D], ALU.subtract).then_inc(step, 1)
            eng.wait_ge(step, 4 * k + 3)
            eng.tensor_copy(sp[:, blk, D:2 * D], sup[:, blk]).then_inc(step, 1)
            eng.wait_ge(step, 4 * k + 4)
            return eng.tensor_tensor(sp[:, blk, 2 * D:W3], sup[:, blk], sp[:, blk, D:2 * D], ALU.subtract)

        @block.sync
        def _(sp_):
            by_block = x[TAIL:N, :].rearrange("(b p) d -> p b d", p=BC)
            for p0, p1 in ((0, 112), (112, BC)):
                sp_.dma_start(xs[1 + p0:1 + p1, 0:BLOCKS], by_block[p0:p1]).then_inc(x_landed, 16)
            sp_.wait_ge(x_zeroed, 2)
            sp_.dma_start(xs[0:TAIL, BLOCKS], x[0:TAIL, :]).then_inc(x_tail_landed, 16)

            with sp_.Fori(0, SUPERS) as s:
                row0 = sp_.snap(s * ROWS)
                for c in range(CHUNKS):
                    if c == BUFS - 1:
                        free = STEPS
                    else:
                        free = (STEPS if c >= BUFS else 0) + GROUPS * CB * ((c - BUFS) % CHUNKS + 1)
                    sp_.wait_ge(tr_done, s * STEPS + free)
                    sp_.nop(nofuse=True)
                    hi = N - c * CB * BC
                    lo = 0 if c == CHUNKS - 1 else hi - CB * BC - 1
                    rows = adj[bass.ds(row0, ROWS), lo:hi]
                    sp_.dma_start(adj_sb[:, c % BUFS, :, CW - (hi - lo):CW], rows.rearrange("(t p) c -> p t c", p=P)
                                  ).then_inc(adj_landed[c % BUFS], 16)
            sp_.wait_ge(adj_landed[0], 16 * SUPERS * CHUNKS // BUFS)
            sp_.sem_inc(adj_landed[0], 16)

        @block.gpsimd
        def _(pool):
            pool.memset(xs[:, BLOCKS], 0.0).then_inc(x_zeroed, 1)
            pool.memset(xs[0:1, 0:BLOCKS], 0.0).then_inc(x_zeroed, 1)
            steps = [0]

            def const(instruction):
                instruction.then_inc(const_step, 1)
                steps[0] += 1
                pool.wait_ge(const_step, steps[0])

            def diagonal(tile, op, fill, base=0):
                n = tile.shape[1]
                const(pool.affine_select(out=tile, in_=tile, compare_op=op, fill=fill, base=base,
                                         pattern=[[-1, n]], channel_multiplier=1))

            const(pool.memset(ident[:], 0.0))
            diagonal(ident[:], ALU.not_equal, 1.0)
            pool.sem_inc(ident_ready, 1)
            const(pool.memset(ident_h[:], 0.0))
            diagonal(ident_h[:], ALU.not_equal, 1.0)
            const(pool.memset(cnt_w[:], -float(ONE)))
            diagonal(cnt_w[:], ALU.is_gt, 0.0)
            diagonal(cnt_w[:], ALU.not_equal, float(FULL))
            const(pool.memset(cnt_w[0:1, :], -1.0))
            const(pool.memset(cnt_w[:, 0:1], float(ONE)))
            const(pool.memset(cnt_w[0:1, 0:1], 1.0))
            const(pool.memset(cnt_tail[:], -float(ONE)))
            diagonal(cnt_tail[:], ALU.is_gt, 0.0)
            diagonal(cnt_tail[:], ALU.not_equal, float(FULL))
            const(pool.memset(cnt_tail[TAIL:TAIL + 1, :], -1.0))
            const(pool.memset(cnt_tail[:, TAIL:P], 0.0))
            const(pool.memset(mask_tail[:], 0.0))
            pool.sem_inc(const_ready, 1)
            pool.wait_ge(norm_step, 11)
            for e in range(1, len(SETS)):
                split(pool, 1, e, e - 1).then_inc(more_parts_ready, 1)
            with pool.Fori(0, SUPERS) as s:
                row0, col0 = pool.snap(s * ROWS), pool.snap(s * (TILES * D))
                pool.wait_ge(out_ready, s + 2)
                pool.nop(nofuse=True)
                pool.dma_start(out[bass.ds(row0, ROWS), :].rearrange("(t p) d -> p t d", p=P),
                               out_sb[:, bass.ds(col0, TILES * D)].rearrange("p (t d) -> p t d", d=D)
                               ).then_inc(out_landed, 16)
            pool.wait_ge(out_landed, 16 * SUPERS)

        @block.scalar
        def _(act):
            act.dma_start(w_sb[:], weight).then_inc(w_landed, 16)
            act.dma_start(bias_sb[:], bias.rearrange("(a d) -> a d", a=1).broadcast_to([P, D])).then_inc(small_landed, 16)
            act.dma_start(xb[:].rearrange("p (t d) -> p t d", d=D), x.rearrange("(t p) d -> p t d", p=P)
                          ).then_inc(small_landed, 16)
            def bring(e):
                b0, nb = SETS[e]
                act.wait_ge(sup_product, e + 1)
                act.copy(sup[:, b0:b0 + nb], acc_ps[:, e % 4, 0:nb * D].rearrange("p (b d) -> p b d", d=D)
                         ).then_inc(sup_ready, 1)

            for i, (b, n) in enumerate(HALVES):
                act.wait_ge(xc_transposed, i + 1)
                act.activation(h_t[:, b:b + n], cnt_ps[0:D, i % 2, 0:n * P].rearrange("p (t r) -> p t r", r=P),
                               ACT.Relu).then_inc(ht_ready, 1)
                if i >= 2 and i % 2 == 0:
                    bring(i // 2 - 1)
                if i == 5:
                    act.wait_ge(norm_step, 6)
                    act.activation(stat[:, 3], stat[:, 2], ACT.Sqrt).then_inc(root_ready, 1)
            bring(len(SETS) - 1)

            with act.Fori(0, SUPERS) as s:
                def encode(n, t, dst):
                    for g in range(GROUPS):
                        act.wait_ge(counted, s * STEPS + n * GROUPS + g + 1)
                        cols = slice(g * GR, (g + 1) * GR)
                        act.activation(dst[:, cols].bitcast(I16), cnt_ps[0:dst.shape[0], g], ACT.Relu
                                       ).then_inc(wts_ready, 1)

                with act.Fori(0, LOOPS) as q:
                    for t in range(LB):
                        encode(q * LB + t, t, wts[:, t % 2])
                encode(BLOCKS, 0, wts_tail[:])

        @block.vector
        def _(dve):
            dve.sem_inc(mask_ready, GROUPS)
            dve.sem_inc(acc_read, TILES // 2)
            dve.sem_inc(out_ready, 1)

            def group(tile, g):
                return tile[:, g * GR:(g + 1) * GR]

            def masks(base, n, t, g):
                dve.wait_ge(tr_done, base + (STEPS + n * GROUPS + g + 1))
                dst, rows = (mask_tail, TAIL) if t is None else (mask_t[:, t % 2], P)
                dve.tensor_scalar(dst[0:rows, g * GR:(g + 1) * GR], tr_ps[g][0:rows, 0:GR], 0.0, None, ALU.not_equal
                                  ).then_inc(mask_ready, 1)

            def carry(base, n, t, g, tail=False):
                dve.wait_ge(mask_ready, base + ((n + 2) * GROUPS + g + 1))
                dve.wait_ge(wts_ready, base + (n * GROUPS + g + 1))
                dst = mask_tail[TAIL:TAIL + 1] if tail else mask_t[0:1, (t + 1) % 2]
                dve.tensor_scalar(dst[:, g * GR:(g + 1) * GR], wts[0:1, t % 2, g * GR:(g + 1) * GR].bitcast(I16),
                                  float(FULL), None, ALU.min).then_inc(carry_ready, 1)

            def no_carry(g):
                dve.memset(mask_t[0:1, 0, g * GR:(g + 1) * GR], 0.0).then_inc(carry_ready, 1)

            dve.wait_ge(x_landed, 32)
            dve.wait_ge(x_tail_landed, 16)
            dve.tensor_reduce(stat[:, 0], xs[:], X, ALU.add).then_inc(norm_step, 1)
            dve.wait_ge(norm_step, 1)
            dve.tensor_scalar(stat[:, 1], stat[:, 0], 1.0 / D, None, ALU.mult).then_inc(norm_step, 1)
            dve.wait_ge(norm_step, 2)
            dve.tensor_tensor(xc[:], xs[:], per_row(stat[:, 1], D), ALU.subtract).then_inc(norm_step, 1)
            dve.wait_ge(norm_step, 3)
            dve.tensor_tensor(sq[:], xc[:], xc[:], ALU.mult).then_inc(norm_step, 1)
            dve.wait_ge(norm_step, 4)
            dve.tensor_reduce(stat[:, 0], sq[:], X, ALU.add).then_inc(norm_step, 1)
            dve.wait_ge(norm_step, 5)
            dve.tensor_scalar(stat[:, 2], stat[:, 0], 1.0 / D, EPS, ALU.mult, ALU.add).then_inc(norm_step, 1)
            dve.wait_ge(root_ready, 1)
            dve.reciprocal(stat[:, 4], stat[:, 3]).then_inc(norm_step, 1)
            dve.wait_ge(norm_step, 7)
            dve.tensor_tensor(stat[:, 5], stat[:, 4], stat[:, 4], ALU.mult).then_inc(norm_step, 1)
            dve.wait_ge(norm_step, 8)
            dve.tensor_tensor(stat[:, 6], stat[:, 5], stat[:, 2], ALU.mult).then_inc(norm_step, 1)
            dve.wait_ge(norm_step, 9)
            dve.tensor_scalar(stat[:, 5], stat[:, 6], -0.5 * 2 ** SHIFT, 1.5 * 2 ** SHIFT, ALU.mult, ALU.add
                              ).then_inc(norm_step, 1)
            dve.wait_ge(norm_step, 10)
            dve.tensor_tensor(stat[:, 7], stat[:, 5], stat[:, 4], ALU.mult).then_inc(norm_step, 1)
            dve.wait_ge(norm_step, 11)
            split(dve, 0, 0, 0).then_inc(first_parts_ready, 1)
            dve.wait_ge(const_ready, 1)
            for t in range(2):
                for g in range(GROUPS):
                    masks(0, t, t, g)
            for g in range(GROUPS):
                dve.wait_ge(mask_ready, GROUPS + g + 1)
                no_carry(g)
            dve.wait_ge(small_landed, 32)
            x3 = xb[:].rearrange("p (t d) -> p t d", d=D)
            dve.tensor_tensor(x3, x3, bias_sb[:].unsqueeze(1).broadcast_to([P, XT, D]), ALU.add).then_inc(norm_step, 1)

            with dve.Fori(0, SUPERS) as s:
                base = s * STEPS
                with dve.Fori(0, LOOPS - 1) as q:
                    inner = base + q * (LB * GROUPS)
                    for t in range(LB):
                        for g in range(GROUPS):
                            carry(inner, t, t, g)
                            masks(inner, t + 2, t, g)
                for t in range(LB):
                    n = BLOCKS - LB + t
                    for g in range(GROUPS):
                        carry(base, n, t, g, tail=t == LB - 1)
                        if t < LB - 2:
                            masks(base, n + 2, t, g)
                        elif t == LB - 2:
                            masks(base, BLOCKS, None, g)
                        else:
                            masks(base, ALL, 0, g)
                for g in range(GROUPS):
                    dve.wait_ge(mask_ready, base + (STEPS + GROUPS + g + 1))
                    no_carry(g)
                for g in range(GROUPS):
                    masks(base, ALL + 1, 1, g)
                cols = bass.ds(dve.snap(s * (TILES * D)), TILES * D)
                dve.wait_ge(product_done, s + 1)
                dve.wait_ge(out_ready, s + 1)
                for a in range(TILES // 2):
                    dve.tensor_reduce(red[:, 2 * a:2 * a + 2],
                                      acc_ps[:, a, 0:2 * W3].rearrange("p (t k d) -> p t d k", t=2, d=D),
                                      X, ALU.add).then_inc(acc_read, 1)
                dve.wait_ge(acc_read, s * (TILES // 2) + TILES)
                dve.tensor_tensor(out_sb[:, cols], red[:].rearrange("p t d -> p (t d)"), xb[:, cols], ALU.add
                                  ).then_inc(out_ready, 1)

        @block.tensor
        def _(pe):
            pe.sem_inc(tr_done, STEPS)

            pe.wait_ge(norm_step, 3)
            pe.wait_ge(ident_ready, 1)
            pe.wait_ge(w_landed, 16)
            for i in range(len(HALVES) + 1):
                if i < len(HALVES):
                    if i >= 2:
                        pe.wait_ge(ht_ready, i - 1)
                    b, n = HALVES[i]
                    for t in range(n):
                        last = pe.transpose(cnt_ps[0:D, i % 2, t * P:(t + 1) * P], xc[:, b + t], ident[:])
                    last.then_inc(xc_transposed, 1)
                if i:
                    b, n = HALVES[i - 1]
                    e, b0 = (i - 1) // 2, SETS[(i - 1) // 2][0]
                    pe.wait_ge(ht_ready, i)
                    if e >= 4:
                        pe.wait_ge(sup_ready, e - 3)
                    for t in range(b, b + n):
                        last = pe.matmul(acc_ps[:, e % 4, (t - b0) * D:(t - b0 + 1) * D], h_t[:, t], w_sb[:],
                                         start=True, stop=True)
                    if b == b0:
                        last.then_inc(sup_product, 1)

            def transpose(base, landed, n, t, g):
                if t is not None and t % CB == 0 and g == 0:
                    pe.wait_ge(adj_landed[t // CB], landed)
                pe.wait_ge(mask_ready, base + (n * GROUPS + g + 1))
                if t is None:
                    buf, col = BUFS - 1, 0
                else:
                    buf, col = t // CB, TAIL - 1 + (CB - 1 - t % CB) * BC
                for i in range(GT):
                    words = adj_sb[:, buf, g * GT + i, col:col + P].bitcast(BF16).rearrange("p (c h) -> p c h", h=2)
                    last = pe.transpose(tr_ps[g][:, i * P:(i + 1) * P], words[:, :, 1], ident_h[:])
                last.then_inc(tr_done, 1)

            def count(base, n, t, g):
                pe.wait_ge(carry_ready, base + (n * GROUPS + g + 1))
                if t is None:
                    mm = pe.matmul(cnt_ps[:, g], cnt_tail[:], mask_tail[:, g * GR:(g + 1) * GR],
                                   start=True, stop=True)
                else:
                    mm = pe.matmul(cnt_ps[:, g], cnt_w[:], mask_t[:, t % 2, g * GR:(g + 1) * GR],
                                   start=True, stop=True)
                mm.then_inc(counted, 1)

            def product(b, t, g, first=False):
                for i in range(g * GT, (g + 1) * GT):
                    if t is None:
                        lhs, rhs = wts_tail[:, i * P:(i + 1) * P], sp[:, b]
                    else:
                        lhs, rhs = wts[:, t % 2, i * P:(i + 1) * P], sp[:, b]
                    last = pe.matmul(acc_ps[:, i // 2, (i % 2) * W3:(i % 2 + 1) * W3], lhs, rhs,
                                     start=first and i % 2 == 0, stop=True, skip_group_check=True)
                return last

            pe.wait_ge(const_ready, 1)
            for t in range(2):
                for g in range(GROUPS):
                    transpose(0, 16, t, t, g)
            pe.wait_ge(first_parts_ready, 1)
            pe.wait_ge(sup_ready, len(SETS))
            with pe.Fori(0, SUPERS) as s:
                base = s * STEPS
                lands = s * (16 * CHUNKS // BUFS)
                for t in range(LB):
                    if t == 1:
                        pe.wait_ge(acc_read, s * (TILES // 2) + TILES // 2)
                    for g in range(GROUPS):
                        count(base, t, t, g)
                        if t:
                            product(BLOCKS - t, t - 1, g, first=t == 1)
                        transpose(base, lands + (16 if t + 2 < LB else 32), t + 2, (t + 2) % LB, g)
                with pe.Fori(1, LOOPS - 1) as q:
                    inner = base + q * (LB * GROUPS)
                    for t in range(LB):
                        if t == 1:
                            pe.wait_ge(more_parts_ready, q)
                        for g in range(GROUPS):
                            count(inner, t, t, g)
                            product((BLOCKS - t) - q * LB, t - 1, g)
                            transpose(inner, lands + q * 16 + (16 if t + 2 < LB else 32), t + 2, (t + 2) % LB, g)
                for t in range(LB):
                    n = BLOCKS - LB + t
                    if t == 1:
                        pe.wait_ge(more_parts_ready, len(SETS) - 1)
                    for g in range(GROUPS):
                        count(base, n, t, g)
                        product(BLOCKS - n, t - 1, g)
                        if t < LB - 2:
                            transpose(base, lands + 16 * LOOPS, n + 2, t + 2, g)
                        elif t == LB - 2:
                            transpose(base, None, BLOCKS, None, g)
                        else:
                            transpose(base, lands + 16 * (LOOPS + 1), ALL, 0, g)
                for g in range(GROUPS):
                    count(base, BLOCKS, None, g)
                    product(0, LB - 1, g)
                    transpose(base, None, ALL + 1, 1, g)
                for g in range(GROUPS):
                    pe.wait_ge(wts_ready, base + (STEPS - GROUPS + g + 1))
                    last = product(BLOCKS, None, g)
                last.then_inc(product_done, 1)


def per_row(ap, n):
    return ap.unsqueeze(2).broadcast_to([ap.shape[0], ap.shape[1], n])


_INS = ["x", "adj", "L0_gnn_weight", "L0_gnn_bias"]


def kernel(**inputs):
    import numpy as np
    import concourse.bacc as bacc
    from concourse.bass_utils import run_bass_kernel_spmd as run

    nc = bacc.Bacc("TRN2", target_bir_lowering=False, num_devices=1)
    arrays, args = {}, []
    for name in _INS:
        a = np.ascontiguousarray(inputs[name])
        arrays[f"in_{name}"] = a
        args.append(nc.dram_tensor(f"in_{name}", a.shape, mybir.dt.from_np(a.dtype), kind="ExternalInput").ap())
    args.append(nc.dram_tensor("out_x", inputs["x"].shape, mybir.dt.float32, kind="ExternalOutput").ap())
    decayed_neighbour_layer(nc, *args)
    return run(nc, [arrays], core_ids=[0]).results[0]["out_x"]
```

```python
from contextlib import ExitStack

import concourse.bass as bass
from concourse import mybir
from concourse.alu_op_type import AluOpType as ALU

P = 128
MAX_NEIGH = 100
EPS = 1e-5
PARTS = 3


def decayed_neighbour_layer(nc, x, adj, weight, bias, out):
    F32, BF16, I16 = mybir.dt.float32, mybir.dt.bfloat16, mybir.dt.int16
    ACT = mybir.ActivationFunctionType
    X = mybir.AxisListType.X

    N, D = x.shape
    TILES = 8
    GROUPS = 2
    GT = TILES // GROUPS
    GR = GT * P
    ROWS = TILES * P
    SUPERS = N // ROWS
    BC = P - 1
    BLOCKS = N // BC
    TAIL = N - BLOCKS * BC
    CB = 2
    BUFS = 4
    CHUNKS = BLOCKS // CB
    CW = TAIL + CB * BC
    LB = BUFS * CB
    LOOPS = BLOCKS // LB
    ALL = BLOCKS + 1
    STEPS = GROUPS * ALL
    W3 = PARTS * D
    ONE = 1 << 7
    FULL = MAX_NEIGH * ONE
    SHIFT = 127 - MAX_NEIGH
    XT = N // P
    SETS = [(b, LB) for b in range(ALL - LB, 0, -LB)] + [(0, 1)]
    EARLY = 2
    PIECES = [slice(SETS[EARLY - 1][0], ALL), slice(0, SETS[EARLY - 1][0])]
    FIRST = 4
    WARM_UPS = 9
    POOL_SETS = (2, 3)
    assert TAIL == 32 and BLOCKS % LB == 0

    ctx = ExitStack()
    with ctx:
        def sb(name, shape, dt):
            return ctx.enter_context(nc.sbuf_tensor(name, shape, dt))

        def sem(name):
            return ctx.enter_context(nc.semaphore(name))

        adj_sb = sb("adj_sb", [P, BUFS, TILES, CW], F32)
        mask_t = sb("mask_t", [P, 2, ROWS], BF16)
        mask_tail = sb("mask_tail", [P, ROWS], BF16)
        wts = sb("wts", [P, 2, ROWS], BF16)
        wts_tail = sb("wts_tail", [P, ROWS], BF16)
        sp = sb("sp", [P, ALL, W3], BF16)
        xs = sb("xs", [P, ALL, D], F32)
        xb = sb("xb", [P, XT * D], F32)
        xc = sb("xc", [P, ALL, D], F32)
        sq = sb("sq", [P, ALL, D], F32)
        h_t = sb("h_t", [P, 2, LB // 2, P], F32)
        sup = sb("sup", [P, ALL, D], F32)
        acc_sb = sb("acc_sb", [P, TILES, PARTS, D], F32)
        out_sb = sb("out_sb", [P, XT * D], F32)
        stat = sb("stat", [P, 8, ALL], F32)
        bias_sb = sb("bias_sb", [P, D], F32)
        w2 = sb("w2", [P, P], F32)
        ident = sb("ident", [P, P], F32)
        ident_h = sb("ident_h", [P, P], BF16)
        cnt_w = sb("cnt_w", [P, P], BF16)
        cnt_tail = sb("cnt_tail", [P, P], BF16)

        tr_ps = [ctx.enter_context(nc.psum_tensor(f"tr_ps{g}", [P, 1024], BF16)) for g in range(GROUPS)]
        cnt_ps = ctx.enter_context(nc.psum_tensor("cnt_ps", [P, GROUPS, 512], F32))
        acc_ps = ctx.enter_context(nc.psum_tensor("acc_ps", [P, TILES // 2, 512], F32))

        x_zeroed = sem("x_zeroed")
        rows_zeroed = sem("rows_zeroed")
        mask_tail_zeroed = sem("mask_tail_zeroed")
        warm = sem("warm")
        x_landed = [sem(f"x_landed{i}") for i in range(3)]
        x_tail_landed = sem("x_tail_landed")
        small_landed = sem("small_landed")
        adj_landed = [sem(f"adj_landed{i}") for i in range(BUFS)]
        out_landed = sem("out_landed")
        last_out_landed = sem("last_out_landed")
        const_step = sem("const_step")
        ident_ready = sem("ident_ready")
        const_ready = sem("const_ready")
        w_zeroed = sem("w_zeroed")
        w_landed = sem("w_landed")
        mean_step = sem("mean_step")
        centred = [sem(f"centred{e}") for e in range(len(SETS))]
        squared = sem("squared")
        summed = sem("summed")
        norm_step = [sem("norm_step0"), sem("norm_step1")]
        root_ready = sem("root_ready")
        xc_transposed = sem("xc_transposed")
        ht_ready = sem("ht_ready")
        sup_product = sem("sup_product")
        sup_ready = sem("sup_ready")
        split_step = [sem("split_step0"), sem("split_step1")]
        first_parts_ready = sem("first_parts_ready")
        more_parts_ready = sem("more_parts_ready")
        tr_done = sem("tr_done")
        first_masks_ready = sem("first_masks_ready")
        carry_ready = sem("carry_ready")
        counted = sem("counted")
        wts_ready = sem("wts_ready")
        product_done = [sem("product_done0"), sem("product_done1")]
        acc_read = [sem("acc_read0"), sem("acc_read1")]
        xb_ready = sem("xb_ready")
        pool_sum = sem("pool_sum")
        last_sum = sem("last_sum")

        block = ctx.enter_context(nc.Block())

        def of_set(e):
            return slice(SETS[e][0], sum(SETS[e]))

        def centre(eng, e):
            eng.wait_ge(mean_step, 2 * e + 2)
            eng.tensor_tensor(xc[:, of_set(e)], xs[:, of_set(e)], per_row(stat[:, 1, of_set(e)], D), ALU.subtract
                              ).then_inc(centred[e], 1)

        def early(e):
            return 0 if e < EARLY else 1

        def refine(eng, i):
            at, step = PIECES[i], norm_step[i]
            eng.wait_ge(step, 2)
            eng.tensor_tensor(stat[:, 5, at], stat[:, 4, at], stat[:, 4, at], ALU.mult).then_inc(step, 1)
            eng.wait_ge(step, 3)
            eng.tensor_tensor(stat[:, 6, at], stat[:, 5, at], stat[:, 2, at], ALU.mult).then_inc(step, 1)
            eng.wait_ge(step, 4)
            eng.tensor_scalar(stat[:, 5, at], stat[:, 6, at], -0.5 * 2 ** SHIFT, 1.5 * 2 ** SHIFT, ALU.mult, ALU.add
                              ).then_inc(step, 1)
            eng.wait_ge(step, 5)
            eng.tensor_tensor(stat[:, 7, at], stat[:, 5, at], stat[:, 4, at], ALU.mult).then_inc(step, 1)

        def split(eng, who, e, k, blk):
            step = split_step[who]
            eng.wait_ge(norm_step[early(e)], 6)
            eng.wait_ge(sup_ready, e + 1)
            eng.tensor_tensor(sup[:, blk], sup[:, blk], per_row(stat[:, 7, blk], D), ALU.mult).then_inc(step, 1)
            eng.wait_ge(step, 4 * k + 1)
            eng.tensor_copy(sp[:, blk, 0:D], sup[:, blk]).then_inc(step, 1)
            eng.wait_ge(step, 4 * k + 2)
            eng.tensor_tensor(sup[:, blk], sup[:, blk], sp[:, blk, 0:D], ALU.subtract).then_inc(step, 1)
            eng.wait_ge(step, 4 * k + 3)
            eng.tensor_copy(sp[:, blk, D:2 * D], sup[:, blk]).then_inc(step, 1)
            eng.wait_ge(step, 4 * k + 4)
            return eng.tensor_tensor(sp[:, blk, 2 * D:W3], sup[:, blk], sp[:, blk, D:2 * D], ALU.subtract)

        @block.sync
        def _(sp_):
            by_block = x[TAIL:N, :].rearrange("(b p) d -> p b d", p=BC)
            for i, blocks in enumerate((slice(BLOCKS - LB, BLOCKS), slice(BLOCKS - 2 * LB, BLOCKS - LB),
                                        slice(0, BLOCKS - 2 * LB))):
                for p0, p1 in ((0, 112), (112, BC)):
                    sp_.dma_start(xs[1 + p0:1 + p1, 1 + blocks.start:1 + blocks.stop], by_block[p0:p1, blocks]
                                  ).then_inc(x_landed[i], 16)
            sp_.wait_ge(x_zeroed, 2)
            sp_.dma_start(xs[0:TAIL, 0], x[0:TAIL, :]).then_inc(x_tail_landed, 16)

            with sp_.Fori(0, SUPERS) as s:
                row0 = sp_.snap(s * ROWS)
                for c in range(CHUNKS):
                    if c == BUFS - 1:
                        free = STEPS
                    else:
                        free = (STEPS if c >= BUFS else 0) + GROUPS * CB * ((c - BUFS) % CHUNKS + 1)
                    sp_.wait_ge(tr_done, s * STEPS + free)
                    sp_.nop(nofuse=True)
                    hi = N - c * CB * BC
                    lo = 0 if c == CHUNKS - 1 else hi - CB * BC - 1
                    rows = adj[bass.ds(row0, ROWS), lo:hi]
                    sp_.dma_start(adj_sb[:, c % BUFS, :, CW - (hi - lo):CW], rows.rearrange("(p t) c -> p t c", p=P)
                                  ).then_inc(adj_landed[c % BUFS], 16)
            sp_.wait_ge(adj_landed[0], 16 * SUPERS * CHUNKS // BUFS)
            sp_.sem_inc(adj_landed[0], 16)
            for g in range(GROUPS):
                t0 = (SUPERS - 1) * TILES + g * GT
                sp_.wait_ge(last_sum, GROUPS * (PARTS - 1) + g + 1)
                sp_.dma_start(out[N - ROWS:N, :].rearrange("(p t) d -> p t d", p=P)[:, g * GT:(g + 1) * GT],
                              out_sb[:, t0 * D:(t0 + GT) * D].rearrange("p (t d) -> p t d", d=D)
                              ).then_inc(last_out_landed, 16)
            sp_.wait_ge(last_out_landed, 16 * GROUPS)

        @block.gpsimd
        def _(pool):
            pool.sem_inc(pool_sum, 1)
            pool.memset(w2[:], 0.0).then_inc(w_zeroed, 1)
            pool.memset(xs[0:1, 1:ALL - LB], 0.0).then_inc(rows_zeroed, 1)
            steps = [0]

            def const(instruction):
                instruction.then_inc(const_step, 1)
                steps[0] += 1
                pool.wait_ge(const_step, steps[0])

            def diagonal(tile, op, fill):
                n = tile.shape[1]
                const(pool.affine_select(out=tile, in_=tile, compare_op=op, fill=fill, base=0,
                                         pattern=[[-1, n]], channel_multiplier=1))

            const(pool.memset(ident[:], 0.0))
            diagonal(ident[:], ALU.not_equal, 1.0)
            pool.sem_inc(ident_ready, 1)
            const(pool.memset(ident_h[:], 0.0))
            diagonal(ident_h[:], ALU.not_equal, 1.0)
            const(pool.memset(cnt_w[:], -float(ONE)))
            diagonal(cnt_w[:], ALU.is_gt, 0.0)
            diagonal(cnt_w[:], ALU.not_equal, float(FULL))
            const(pool.memset(cnt_w[0:1, :], -1.0))
            const(pool.memset(cnt_w[:, 0:1], float(ONE)))
            const(pool.memset(cnt_w[0:1, 0:1], 1.0))
            const(pool.memset(cnt_tail[:], -float(ONE)))
            diagonal(cnt_tail[:], ALU.is_gt, 0.0)
            diagonal(cnt_tail[:], ALU.not_equal, float(FULL))
            const(pool.memset(cnt_tail[TAIL:TAIL + 1, :], -1.0))
            const(pool.memset(cnt_tail[:, TAIL:P], 0.0))
            pool.sem_inc(const_ready, 1)
            for e in POOL_SETS:
                pool.wait_ge(x_landed[min(e, 2)], 32)
                pool.wait_ge(rows_zeroed, 1)
                centre(pool, e)
            split(pool, 1, 0, 0, slice(SETS[0][0], ALL - FIRST)).then_inc(more_parts_ready, 1)
            split(pool, 1, 1, 1, of_set(1)).then_inc(more_parts_ready, 1)
            pool.dma_start(bias_sb[:], bias.rearrange("(a d) -> a d", a=1).broadcast_to([P, D])).then_inc(small_landed, 16)
            pool.dma_start(xb[:].rearrange("p (s c) -> p s c", s=SUPERS),
                           x.rearrange("(s p t) d -> p s (t d)", p=P, t=TILES)).then_inc(small_landed, 16)
            refine(pool, 1)
            for e in range(2, len(SETS)):
                split(pool, 1, e, e, of_set(e)).then_inc(more_parts_ready, 1)
            pool.wait_ge(small_landed, 32)
            x3 = xb[:].rearrange("p (t d) -> p t d", d=D)
            pool.tensor_tensor(x3, x3, bias_sb[:].unsqueeze(1).broadcast_to([P, XT, D]), ALU.add).then_inc(xb_ready, 1)
            pool.wait_ge(xb_ready, 1)
            with pool.Fori(0, SUPERS - 1) as s:
                row0, col0 = pool.snap(s * ROWS), pool.snap(s * (TILES * D))
                pool.wait_ge(acc_read[0], s + 1)
                pool.wait_ge(acc_read[1], s + 1)
                pool.nop(nofuse=True)
                rows = out_sb[:, bass.ds(col0, TILES * D)].rearrange("p (t d) -> p t d", d=D)
                for k in range(PARTS):
                    other = xb[:, bass.ds(col0, TILES * D)].rearrange("p (t d) -> p t d", d=D) if k == 0 else rows
                    if k:
                        pool.wait_ge(pool_sum, s * PARTS + k + 1)
                        pool.nop(nofuse=True)
                    pool.tensor_tensor(rows, acc_sb[:, :, k], other, ALU.add).then_inc(pool_sum, 1)
                pool.wait_ge(pool_sum, s * PARTS + PARTS + 1)
                pool.nop(nofuse=True)
                pool.dma_start(out[bass.ds(row0, ROWS), :].rearrange("(p t) d -> p t d", p=P), rows
                               ).then_inc(out_landed, 16)
            pool.wait_ge(out_landed, 16 * (SUPERS - 1))

        @block.scalar
        def _(act):
            act.wait_ge(w_zeroed, 1)
            for i in range(2):
                act.dma_start(w2[i * D:(i + 1) * D, i * D:(i + 1) * D], weight).then_inc(w_landed, 16)
            act.wait_ge(warm, 1)
            act.activation(stat[:, 3, 0:1], stat[:, 3, 0:1], ACT.Sqrt).then_inc(warm, 1)

            def square(e):
                act.wait_ge(centred[e], 1)
                act.activation(sq[:, of_set(e)], xc[:, of_set(e)], ACT.Square).then_inc(squared, 1)

            def root(i):
                act.wait_ge(norm_step[i], 1)
                act.wait_ge(warm, 2)
                act.activation(stat[:, 3, PIECES[i]], stat[:, 2, PIECES[i]], ACT.Sqrt).then_inc(root_ready, 1)

            def bring(e):
                b0, nb = SETS[e]
                act.wait_ge(sup_product, e + 1)
                act.copy(sup[:, b0:b0 + nb], acc_ps[:, e % 4, 0:nb * D].rearrange("p (b d) -> p b d", d=D)
                         ).then_inc(sup_ready, 1)

            square(0)
            for e, (b, n) in enumerate(SETS):
                pairs, parts = (n + 1) // 2, P if n > 1 else D
                act.wait_ge(xc_transposed, e + 1)
                act.activation(h_t[0:parts, e % 2, 0:pairs],
                               cnt_ps[0:parts, e % 2, 0:pairs * P].rearrange("p (t r) -> p t r", r=P),
                               ACT.Relu).then_inc(ht_ready, 1)
                if e == 0:
                    square(1)
                else:
                    bring(e - 1)
                if e == 1:
                    root(0)
            bring(len(SETS) - 1)

            def encode(base, n, dst):
                for g in range(GROUPS):
                    act.wait_ge(counted, base + (n * GROUPS + g + 1))
                    cols = slice(g * GR, (g + 1) * GR)
                    act.activation(dst[:, cols].bitcast(I16), cnt_ps[0:dst.shape[0], g], ACT.Relu
                                   ).then_inc(wts_ready, 1)

            def rest_of_row(base):
                with act.Fori(1, LOOPS) as q:
                    for t in range(LB):
                        encode(base + q * (LB * GROUPS), t, wts[:, t % 2])
                encode(base, BLOCKS, wts_tail[:])

            for t in range(LB):
                encode(0, t, wts[:, t % 2])
                if t < len(SETS) - EARLY:
                    square(EARLY + t)
                elif t == len(SETS) - EARLY + 2:
                    root(1)
            with act.Fori(0, SUPERS - 1) as s:
                base = s * STEPS
                rest_of_row(base)
                for t in range(LB):
                    encode(base + STEPS, t, wts[:, t % 2])
                    if t == 0:
                        act.wait_ge(product_done[1], s + 1)
                        act.wait_ge(pool_sum, s * PARTS + 1)
                        act.copy(acc_sb[:, GT:TILES].rearrange("p (a t) k d -> p a (t k d)", a=2),
                                 acc_ps[:, 2:4, 0:2 * W3]).then_inc(acc_read[1], 1)
            rest_of_row((SUPERS - 1) * STEPS)

        @block.vector
        def _(dve):
            def masks(base, n, t, g):
                dve.wait_ge(tr_done, base + (STEPS + n * GROUPS + g + 1))
                dst, rows = (mask_tail, TAIL) if t is None else (mask_t[:, t % 2], P)
                return dve.tensor_scalar(dst[0:rows, g * GR:(g + 1) * GR], tr_ps[g][0:rows, 0:GR], 0.0, None,
                                         ALU.not_equal)

            def carry(base, n, t, g, tail=False):
                dve.wait_ge(wts_ready, base + (n * GROUPS + g + 1))
                dst = mask_tail[TAIL:TAIL + 1] if tail else mask_t[0:1, (t + 1) % 2]
                dve.tensor_scalar(dst[:, g * GR:(g + 1) * GR], wts[0:1, t % 2, g * GR:(g + 1) * GR].bitcast(I16),
                                  float(FULL), None, ALU.min).then_inc(carry_ready, 1)

            def no_carry(g):
                dve.memset(mask_t[0:1, 0, g * GR:(g + 1) * GR], 0.0).then_inc(carry_ready, 1)

            def mean(e):
                at = of_set(e)
                if e == 0:
                    dve.wait_ge(x_landed[0], 32)
                    dve.wait_ge(x_zeroed, 1)
                elif SETS[e][0] > 0:
                    dve.wait_ge(x_landed[min(e, 2)], 32)
                    dve.wait_ge(rows_zeroed, 1)
                else:
                    dve.wait_ge(x_tail_landed, 16)
                    dve.wait_ge(x_zeroed, 2)
                dve.tensor_reduce(stat[:, 0, at], xs[:, at], X, ALU.add).then_inc(mean_step, 1)
                dve.wait_ge(mean_step, 2 * e + 1)
                dve.tensor_scalar(stat[:, 1, at], stat[:, 0, at], 1.0 / D, None, ALU.mult).then_inc(mean_step, 1)

            def sum_squares(e):
                dve.wait_ge(squared, e + 1)
                dve.tensor_reduce(stat[:, 6, of_set(e)], sq[:, of_set(e)], X, ALU.add).then_inc(summed, 1)

            def variance(i):
                at = PIECES[i]
                dve.wait_ge(summed, len(SETS) if i else EARLY)
                dve.tensor_scalar(stat[:, 2, at], stat[:, 6, at], 1.0 / D, EPS, ALU.mult, ALU.add
                                  ).then_inc(norm_step[i], 1)

            def inverse(i):
                dve.wait_ge(root_ready, i + 1)
                dve.reciprocal(stat[:, 4, PIECES[i]], stat[:, 3, PIECES[i]]).then_inc(norm_step[i], 1)

            dve.memset(mask_tail[:], 0.0).then_inc(mask_tail_zeroed, 1)
            dve.memset(xs[0:1, ALL - LB:ALL], 0.0).then_inc(x_zeroed, 1)
            dve.memset(xs[:, 0], 0.0).then_inc(x_zeroed, 1)
            dve.memset(stat[:, 3, 0:1], 1.0).then_inc(warm, 1)

            for e in range(EARLY):
                mean(e)
                centre(dve, e)
            for e in range(EARLY):
                sum_squares(e)
            for e in range(EARLY, len(SETS)):
                mean(e)
            variance(0)
            centre(dve, len(SETS) - 1)
            inverse(0)
            refine(dve, 0)
            split(dve, 0, 0, 0, slice(ALL - FIRST, ALL)).then_inc(first_parts_ready, 1)
            for t in range(2):
                for g in range(GROUPS):
                    masks(0, t, t, g).then_inc(first_masks_ready, 1)
                if t == 0:
                    for g in range(GROUPS):
                        dve.wait_ge(first_masks_ready, g + 1)
                        no_carry(g)
            dve.wait_ge(mask_tail_zeroed, 1)

            def rest_of_row(base):
                with dve.Fori(1, LOOPS - 1) as q:
                    inner = base + q * (LB * GROUPS)
                    for t in range(LB):
                        for g in range(GROUPS):
                            masks(inner, t + 2, t, g)
                            carry(inner, t, t, g)
                for t in range(LB):
                    n = BLOCKS - LB + t
                    for g in range(GROUPS):
                        if t < LB - 2:
                            masks(base, n + 2, t, g)
                        elif t == LB - 2:
                            masks(base, BLOCKS, None, g)
                        else:
                            masks(base, ALL, 0, g)
                        carry(base, n, t, g, tail=t == LB - 1)
                for g in range(GROUPS):
                    masks(base, ALL + 1, 1, g)
                    no_carry(g)

            for t in range(LB):
                for g in range(GROUPS):
                    masks(0, t + 2, t, g)
                    carry(0, t, t, g)
                if 1 <= t <= len(SETS) - EARLY:
                    sum_squares(EARLY + t - 1)
                elif t == len(SETS) - EARLY + 1:
                    variance(1)
                elif t == len(SETS) - EARLY + 3:
                    inverse(1)
            with dve.Fori(0, SUPERS - 1) as s:
                base = s * STEPS
                rest_of_row(base)
                for t in range(LB):
                    for g in range(GROUPS):
                        masks(base + STEPS, t + 2, t, g)
                        carry(base + STEPS, t, t, g)
                        if t == 0 and g == 0:
                            dve.wait_ge(product_done[0], s + 1)
                            dve.wait_ge(pool_sum, s * PARTS + 1)
                            dve.tensor_copy(acc_sb[:, 0:GT].rearrange("p (a t) k d -> p a (t k d)", a=2),
                                            acc_ps[:, 0:2, 0:2 * W3]).then_inc(acc_read[0], 1)
            rest_of_row((SUPERS - 1) * STEPS)
            dve.wait_ge(xb_ready, 1)
            for k in range(PARTS):
                for g in range(GROUPS):
                    t0 = (SUPERS - 1) * TILES + g * GT
                    cols = slice(t0 * D, (t0 + GT) * D)
                    half = out_sb[:, cols].rearrange("p (a t d) -> p a t d", a=2, d=D)
                    part = acc_ps[:, 2 * g:2 * g + 2, 0:2 * W3].rearrange("p a (t k d) -> p a t k d", t=2, d=D
                                                                         )[:, :, :, k]
                    if k == 0:
                        dve.wait_ge(product_done[g], SUPERS)
                        other = xb[:, cols].rearrange("p (a t d) -> p a t d", a=2, d=D)
                    else:
                        dve.wait_ge(last_sum, GROUPS * (k - 1) + g + 1)
                        other = half
                    dve.tensor_tensor(half, part, other, ALU.add).then_inc(last_sum, 1)

        @block.tensor
        def _(pe):
            pe.sem_inc(tr_done, STEPS)

            pe.wait_ge(mask_tail_zeroed, 1)
            for _ in range(WARM_UPS):
                pe.matmul(acc_ps[:, 3], mask_tail[:, 0:P], mask_tail[:, 0:GR], start=True, stop=True)

            pe.wait_ge(ident_ready, 1)

            def transpose_set(e):
                b, n = SETS[e]
                pe.wait_ge(centred[e], 1)
                if e >= 2:
                    pe.wait_ge(ht_ready, e - 1)
                for t in range((n + 1) // 2):
                    k = min(2, n)
                    last = pe.transpose(cnt_ps[0:k * D, e % 2, t * P:(t + 1) * P],
                                        xc[:, b + 2 * t:b + 2 * t + k].rearrange("p b d -> p (b d)"), ident[:])
                last.then_inc(xc_transposed, 1)

            def multiply_set(e):
                b, n = SETS[e]
                pe.wait_ge(ht_ready, e + 1)
                if e >= 4:
                    pe.wait_ge(sup_ready, e - 3)
                for t in range((n + 1) // 2):
                    k = min(2, n)
                    last = pe.matmul(acc_ps[:, e % 4, 2 * t * D:(2 * t + k) * D],
                                     h_t[0:k * D, e % 2, t], w2[0:k * D, 0:k * D], start=True, stop=True)
                last.then_inc(sup_product, 1)

            def transpose(base, landed, n, t, g):
                if t is not None and t % CB == 0 and g == 0:
                    pe.wait_ge(adj_landed[t // CB], landed)
                if t is None:
                    buf, col = BUFS - 1, 0
                else:
                    buf, col = t // CB, TAIL - 1 + (CB - 1 - t % CB) * BC
                for i in range(GT):
                    words = adj_sb[:, buf, g * GT + i, col:col + P].bitcast(BF16).rearrange("p (c h) -> p c h", h=2)
                    last = pe.transpose(tr_ps[g][:, i * P:(i + 1) * P], words[:, :, 1], ident_h[:])
                last.then_inc(tr_done, 1)

            def count(base, n, t, g):
                pe.wait_ge(carry_ready, base + (n * GROUPS + g + 1))
                if t is None:
                    mm = pe.matmul(cnt_ps[:, g], cnt_tail[:], mask_tail[:, g * GR:(g + 1) * GR],
                                   start=True, stop=True)
                else:
                    mm = pe.matmul(cnt_ps[:, g], cnt_w[:], mask_t[:, t % 2, g * GR:(g + 1) * GR],
                                   start=True, stop=True)
                mm.then_inc(counted, 1)

            def product(b, t, g, first=False):
                for i in range(g * GT, (g + 1) * GT):
                    if t is None:
                        lhs, rhs = wts_tail[:, i * P:(i + 1) * P], sp[:, b]
                    else:
                        lhs, rhs = wts[:, t % 2, i * P:(i + 1) * P], sp[:, b]
                    last = pe.matmul(acc_ps[:, i // 2, (i % 2) * W3:(i % 2 + 1) * W3], lhs, rhs,
                                     start=first and i % 2 == 0, stop=True, skip_group_check=True)
                return last

            def first_transposes(t):
                for g in range(GROUPS):
                    if t:
                        pe.wait_ge(first_masks_ready, g + 1)
                    transpose(0, 16, t, t, g)

            transpose_set(0)
            pe.wait_ge(w_landed, 32)
            multiply_set(0)
            transpose_set(1)
            multiply_set(1)
            transpose_set(2)
            transpose_set(3)
            multiply_set(2)
            pe.wait_ge(const_ready, 1)
            first_transposes(0)
            multiply_set(3)
            transpose_set(4)
            first_transposes(1)
            multiply_set(4)
            def first_body(base, lands, after=None):
                for t in range(LB):
                    for g in range(GROUPS):
                        if t == 0 and after is not None:
                            pe.wait_ge(wts_ready, base + (g - GROUPS + 1))
                        count(base, t, t, g)
                        if t == 0 and after is None:
                            pe.wait_ge(first_masks_ready, GROUPS + g + 1)
                        transpose(base, lands + (16 if t + 2 < LB else 32), t + 2, (t + 2) % LB, g)
                        if t == 0 and after is not None:
                            product(0, None, g).then_inc(product_done[g], 1)
                        if t == 1 and after is not None:
                            pe.wait_ge(acc_read[g], after)
                        if t == 1 and g == 0:
                            pe.wait_ge(first_parts_ready, 1)
                            pe.wait_ge(sup_ready, len(SETS))
                        elif t == FIRST + 1 and g == 0:
                            pe.wait_ge(more_parts_ready, 1)
                        if t:
                            product(ALL - t, t - 1, g, first=t == 1)

            def rest_of_row(base, lands):
                with pe.Fori(1, LOOPS - 1) as q:
                    inner = base + q * (LB * GROUPS)
                    for t in range(LB):
                        if t == 1:
                            pe.wait_ge(more_parts_ready, q + 1)
                        for g in range(GROUPS):
                            count(inner, t, t, g)
                            transpose(inner, lands + q * 16 + (16 if t + 2 < LB else 32), t + 2, (t + 2) % LB, g)
                            product((ALL - t) - q * LB, t - 1, g)
                for t in range(LB):
                    n = BLOCKS - LB + t
                    if t == 1:
                        pe.wait_ge(more_parts_ready, len(SETS))
                    for g in range(GROUPS):
                        count(base, n, t, g)
                        if t < LB - 2:
                            transpose(base, lands + 16 * LOOPS, n + 2, t + 2, g)
                        elif t == LB - 2:
                            transpose(base, None, BLOCKS, None, g)
                        else:
                            transpose(base, lands + 16 * (LOOPS + 1), ALL, 0, g)
                        product(ALL - n, t - 1, g)
                for g in range(GROUPS):
                    count(base, BLOCKS, None, g)
                    transpose(base, None, ALL + 1, 1, g)
                    product(1, LB - 1, g)

            row_lands = 16 * CHUNKS // BUFS
            first_body(0, 0)
            with pe.Fori(0, SUPERS - 1) as s:
                rest_of_row(s * STEPS, s * row_lands)
                first_body(s * STEPS + STEPS, s * row_lands + row_lands, after=s + 1)
            rest_of_row((SUPERS - 1) * STEPS, (SUPERS - 1) * row_lands)
            for g in range(GROUPS):
                pe.wait_ge(wts_ready, (SUPERS - 1) * STEPS + (STEPS - GROUPS + g + 1))
                product(0, None, g).then_inc(product_done[g], 1)


def per_row(ap, n):
    return ap.unsqueeze(2).broadcast_to([ap.shape[0], ap.shape[1], n])


_INS = ["x", "adj", "L0_gnn_weight", "L0_gnn_bias"]


def kernel(**inputs):
    import numpy as np
    import concourse.bacc as bacc
    from concourse.bass_utils import run_bass_kernel_spmd as run

    nc = bacc.Bacc("TRN2", target_bir_lowering=False, num_devices=1)
    arrays, args = {}, []
    for name in _INS:
        a = np.ascontiguousarray(inputs[name])
        arrays[f"in_{name}"] = a
        args.append(nc.dram_tensor(f"in_{name}", a.shape, mybir.dt.from_np(a.dtype), kind="ExternalInput").ap())
    args.append(nc.dram_tensor("out_x", inputs["x"].shape, mybir.dt.float32, kind="ExternalOutput").ap())
    decayed_neighbour_layer(nc, *args)
    return run(nc, [arrays], core_ids=[0]).results[0]["out_x"]
```
